# Optimizing a Trainium2 kernel written in Bass

```python
import numpy as np
import jax
import jax.numpy as jnp

def _softmax(x, axis=-1):
    return jax.nn.softmax(x, axis=axis)

def _gelu(x):
    return jax.nn.gelu(x, approximate=True)

def _silu(x):
    return jax.nn.silu(x)

def _sigmoid(x):
    return jax.nn.sigmoid(x)

def _layernorm(x, axis=-1, eps=1e-05):
    m = jnp.mean(x, axis=axis, keepdims=True)
    v = jnp.var(x, axis=axis, keepdims=True)
    return (x - m) / jnp.sqrt(v + eps)

def _scatter_add(tgt, idx, src, axis=0):
    return tgt.at[idx].add(src)

def _segment_sum(src, seg, n):
    return jax.ops.segment_sum(src, seg, n)
kernel_name = 'mk_dlrm_tower_d1_rec_r8_d43d44'

def setup_inputs(seed: int=0):
    np.random.seed(seed)
    _w = jnp.asarray

    def _rec_inputs():
        import jax
        import jax.numpy as jnp
        _tk = jax.random.key(seed)
        ids = jnp.stack([jax.random.randint(jax.random.fold_in(_tk, 200 + f), (512,), 0, v, jnp.int32) for f, v in enumerate([12500, 125000, 1000, 1250, 12500, 12500, 1000, 1000, 1000, 1250, 1250, 12500, 12500, 1000, 12500, 1250, 12500, 12500, 12500, 1000, 1000, 1000, 1000, 1000, 1000, 1000])], axis=1)
        tbl_0 = 0.05 * jax.random.normal(jax.random.fold_in(_tk, 500 + 0), (12500, 128), jnp.float32)
        tbl_1 = 0.05 * jax.random.normal(jax.random.fold_in(_tk, 500 + 1), (125000, 128), jnp.float32)
        tbl_2 = 0.05 * jax.random.normal(jax.random.fold_in(_tk, 500 + 2), (1000, 128), jnp.float32)
        tbl_3 = 0.05 * jax.random.normal(jax.random.fold_in(_tk, 500 + 3), (1250, 128), jnp.float32)
        tbl_4 = 0.05 * jax.random.normal(jax.random.fold_in(_tk, 500 + 4), (12500, 128), jnp.float32)
        tbl_5 = 0.05 * jax.random.normal(jax.random.fold_in(_tk, 500 + 5), (12500, 128), jnp.float32)
        tbl_6 = 0.05 * jax.random.normal(jax.random.fold_in(_tk, 500 + 6), (1000, 128), jnp.float32)
        tbl_7 = 0.05 * jax.random.normal(jax.random.fold_in(_tk, 500 + 7), (1000, 128), jnp.float32)
        tbl_8 = 0.05 * jax.random.normal(jax.random.fold_in(_tk, 500 + 8), (1000, 128), jnp.float32)
        tbl_9 = 0.05 * jax.random.normal(jax.random.fold_in(_tk, 500 + 9), (1250, 128), jnp.float32)
        tbl_10 = 0.05 * jax.random.normal(jax.random.fold_in(_tk, 500 + 10), (1250, 128), jnp.float32)
        tbl_11 = 0.05 * jax.random.normal(jax.random.fold_in(_tk, 500 + 11), (12500, 128), jnp.float32)
        tbl_12 = 0.05 * jax.random.normal(jax.random.fold_in(_tk, 500 + 12), (12500, 128), jnp.float32)
        tbl_13 = 0.05 * jax.random.normal(jax.random.fold_in(_tk, 500 + 13), (1000, 128), jnp.float32)
        tbl_14 = 0.05 * jax.random.normal(jax.random.fold_in(_tk, 500 + 14), (12500, 128), jnp.float32)
        tbl_15 = 0.05 * jax.random.normal(jax.random.fold_in(_tk, 500 + 15), (1250, 128), jnp.float32)
        tbl_16 = 0.05 * jax.random.normal(jax.random.fold_in(_tk, 500 + 16), (12500, 128), jnp.float32)
        tbl_17 = 0.05 * jax.random.normal(jax.random.fold_in(_tk, 500 + 17), (12500, 128), jnp.float32)
        tbl_18 = 0.05 * jax.random.normal(jax.random.fold_in(_tk, 500 + 18), (12500, 128), jnp.float32)
        tbl_19 = 0.05 * jax.random.normal(jax.random.fold_in(_tk, 500 + 19), (1000, 128), jnp.float32)
        tbl_20 = 0.05 * jax.random.normal(jax.random.fold_in(_tk, 500 + 20), (1000, 128), jnp.float32)
        tbl_21 = 0.05 * jax.random.normal(jax.random.fold_in(_tk, 500 + 21), (1000, 128), jnp.float32)
        tbl_22 = 0.05 * jax.random.normal(jax.random.fold_in(_tk, 500 + 22), (1000, 128), jnp.float32)
        tbl_23 = 0.05 * jax.random.normal(jax.random.fold_in(_tk, 500 + 23), (1000, 128), jnp.float32)
        tbl_24 = 0.05 * jax.random.normal(jax.random.fold_in(_tk, 500 + 24), (1000, 128), jnp.float32)
        tbl_25 = 0.05 * jax.random.normal(jax.random.fold_in(_tk, 500 + 25), (1000, 128), jnp.float32)
        _rk = jax.random.fold_in(_tk, 7)
        r_bottom_output = -0.000520686 + 1.00062 * jax.random.normal(jax.random.fold_in(_rk, 101), (512, 128), jnp.float32)
        W_top1 = 0.0456912 * jax.random.normal(jax.random.fold_in(_tk, 801), (479, 512), jnp.float32)
        W_top2 = 0.0441942 * jax.random.normal(jax.random.fold_in(_tk, 802), (512, 256), jnp.float32)
        W_top3 = 0.0625 * jax.random.normal(jax.random.fold_in(_tk, 803), (256, 1), jnp.float32)
        b_top1 = jnp.zeros((512,), jnp.float32)
        b_top2 = jnp.zeros((256,), jnp.float32)
        return (r_bottom_output, ids, tbl_0, tbl_1, tbl_2, tbl_3, tbl_4, tbl_5, tbl_6, tbl_7, tbl_8, tbl_9, tbl_10, tbl_11, tbl_12, tbl_13, tbl_14, tbl_15, tbl_16, tbl_17, tbl_18, tbl_19, tbl_20, tbl_21, tbl_22, tbl_23, tbl_24, tbl_25, W_top1, b_top1, W_top2, b_top2, W_top3)
    r_bottom_output, ids, tbl_0, tbl_1, tbl_2, tbl_3, tbl_4, tbl_5, tbl_6, tbl_7, tbl_8, tbl_9, tbl_10, tbl_11, tbl_12, tbl_13, tbl_14, tbl_15, tbl_16, tbl_17, tbl_18, tbl_19, tbl_20, tbl_21, tbl_22, tbl_23, tbl_24, tbl_25, W_top1, b_top1, W_top2, b_top2, W_top3 = _rec_inputs()

    def _L0_rec_setup():
        import jax, jax.numpy as jnp
        import numpy as np
        NUM_FEATURES = 27
        _TRIU_I, _TRIU_J = np.triu_indices(NUM_FEATURES, k=1)
        key = jax.random.key(seed)
        k1, k2 = jax.random.split(key)
        bottom_output = jax.random.normal(k1, (2048, 128), dtype=jnp.float32)
        embeddings = jax.random.normal(k2, (2048, 26, 128), dtype=jnp.float32)
        return {'bottom_output': bottom_output, 'embeddings': embeddings}
    _L0_rec_all = _L0_rec_setup()
    _L0_rec_in = {k: v for k, v in _L0_rec_all.items() if k in ()}
    del _L0_rec_all
    return {'r_bottom_output': r_bottom_output, 'ids': ids, 'tbl_0': tbl_0, 'tbl_1': tbl_1, 'tbl_2': tbl_2, 'tbl_3': tbl_3, 'tbl_4': tbl_4, 'tbl_5': tbl_5, 'tbl_6': tbl_6, 'tbl_7': tbl_7, 'tbl_8': tbl_8, 'tbl_9': tbl_9, 'tbl_10': tbl_10, 'tbl_11': tbl_11, 'tbl_12': tbl_12, 'tbl_13': tbl_13, 'tbl_14': tbl_14, 'tbl_15': tbl_15, 'tbl_16': tbl_16, 'tbl_17': tbl_17, 'tbl_18': tbl_18, 'tbl_19': tbl_19, 'tbl_20': tbl_20, 'tbl_21': tbl_21, 'tbl_22': tbl_22, 'tbl_23': tbl_23, 'tbl_24': tbl_24, 'tbl_25': tbl_25, 'W_top1': W_top1, 'b_top1': b_top1, 'W_top2': W_top2, 'b_top2': b_top2, 'W_top3': W_top3}

def reference(r_bottom_output, ids, tbl_0, tbl_1, tbl_2, tbl_3, tbl_4, tbl_5, tbl_6, tbl_7, tbl_8, tbl_9, tbl_10, tbl_11, tbl_12, tbl_13, tbl_14, tbl_15, tbl_16, tbl_17, tbl_18, tbl_19, tbl_20, tbl_21, tbl_22, tbl_23, tbl_24, tbl_25, W_top1, b_top1, W_top2, b_top2, W_top3):
    import jax
    import jax.numpy as jnp

    def _L0_rec_ref(bottom_output, embeddings):
        import jax, jax.numpy as jnp
        import numpy as np
        NUM_FEATURES = 27
        _TRIU_I, _TRIU_J = np.triu_indices(NUM_FEATURES, k=1)
        all_emb = jnp.concatenate([bottom_output[:, None, :], embeddings], axis=1)
        gram = jnp.einsum('bfd,bgd->bfg', all_emb, all_emb)
        return gram[:, _TRIU_I, _TRIU_J]
    e = jnp.stack([tbl_0[ids[:, 0]], tbl_1[ids[:, 1]], tbl_2[ids[:, 2]], tbl_3[ids[:, 3]], tbl_4[ids[:, 4]], tbl_5[ids[:, 5]], tbl_6[ids[:, 6]], tbl_7[ids[:, 7]], tbl_8[ids[:, 8]], tbl_9[ids[:, 9]], tbl_10[ids[:, 10]], tbl_11[ids[:, 11]], tbl_12[ids[:, 12]], tbl_13[ids[:, 13]], tbl_14[ids[:, 14]], tbl_15[ids[:, 15]], tbl_16[ids[:, 16]], tbl_17[ids[:, 17]], tbl_18[ids[:, 18]], tbl_19[ids[:, 19]], tbl_20[ids[:, 20]], tbl_21[ids[:, 21]], tbl_22[ids[:, 22]], tbl_23[ids[:, 23]], tbl_24[ids[:, 24]], tbl_25[ids[:, 25]]], axis=1)
    z = _L0_rec_ref(r_bottom_output, e)
    z = z.reshape(z.shape[0], -1)
    h = jnp.concatenate([z, r_bottom_output], axis=1)
    h = jnp.maximum(h @ W_top1 + b_top1, 0.0)
    h = jnp.maximum(h @ W_top2 + b_top2, 0.0)
    y = h @ W_top3
    return y

_drawn_inputs = setup_inputs


def setup_inputs(seed=0):
    import zlib

    import numpy as np

    out = dict(_drawn_inputs(seed))
    spreads = {'b_top1': (0.0, 0.1), 'b_top2': (0.0, 0.1)}
    factors = {}
    for name, (base, spread) in spreads.items():
        noise = np.random.default_rng([zlib.crc32(name.encode()), seed]).standard_normal(out[name].shape)
        drawn = base * np.exp(spread * noise) if base else spread * noise
        out[name] = jnp.asarray(drawn.astype(out[name].dtype))
    for name, factor in factors.items():
        out[name] = (out[name] * factor).astype(out[name].dtype)
    return out
```

```python
from contextlib import ExitStack

import concourse.bass as bass
from concourse import mybir

F32 = mybir.dt.float32
I32 = mybir.dt.int32
ALU = mybir.AluOpType
ACT = mybir.ActivationFunctionType

P = 128
B = 512
D = 128
NTAB = 26
NF = NTAB + 1
TILES = B // P
SLOT = 32
QUADS = (NF + 3) // 4
PACK = P // SLOT
HALF = 64
NMM = HALF // PACK
PAIR_COLS = NF - 1
KG = (PAIR_COLS + 3) // 4
H1, H2 = 512, 256
N1, N2 = H1 // P, H2 // P


def quad_slots(q):
    return range(4 * q, min(4 * q + 4, NF))


def build(nc, bottom, ids, tables, w1_pairs, w1_bottom, b1, w2, b2, w3, out):
    ctx = ExitStack()
    with ctx:
        def sb(name, shape, dt=F32):
            return ctx.enter_context(nc.sbuf_tensor(name, shape, dt))

        def ps(name, shape, dt=F32):
            return ctx.enter_context(nc.psum_tensor(name, shape, dt))

        def sem(name):
            return ctx.enter_context(nc.semaphore(name))

        idx = sb("idx", [P, TILES, NTAB], I32)
        emb = sb("emb", [P, TILES, NF, D])
        embT = sb("embT", [P, B, SLOT])
        pairs = sb("pairs", [P, KG, B])
        w1p = sb("w1p", [P, KG, H1])
        w1b = sb("w1b", [P, H1])
        w2s = sb("w2s", [P, N1, H2])
        w3s = sb("w3s", [P, N2])
        b1s = sb("b1s", [P, N1])
        b2s = sb("b2s", [P, N2])
        h1 = sb("h1", [P, TILES, N1, P])
        h2 = sb("h2", [P, TILES, N2, P])
        y = sb("y", [1, B])
        ident = sb("ident", [P, P])

        tr_ps = ps("tr_ps", [P, 2, 4, P])
        gram_ps = ps("gram_ps", [P, NMM, P])
        h1_ps = ps("h1_ps", [P, N1, P])
        h2_ps = ps("h2_ps", [P, 4, P])

        s_idx = sem("s_idx")
        s_bottom = sem("s_bottom")
        s_w1 = sem("s_w1")
        s_w2 = sem("s_w2")
        s_gather = [[sem(f"s_gather_{t}_{q}") for q in range(QUADS)] for t in range(TILES)]
        s_ident0 = sem("s_ident0")
        s_ident = sem("s_ident")
        s_pad = sem("s_pad")
        s_tr = sem("s_tr")
        s_trD = sem("s_trD")
        s_trA = sem("s_trA")
        s_gram = sem("s_gram")
        s_pairD = sem("s_pairD")
        s_pairA = sem("s_pairA")
        s_h1mm = sem("s_h1mm")
        s_h1 = sem("s_h1")
        s_h2mm = sem("s_h2mm")
        s_h2 = sem("s_h2")
        s_ymm = sem("s_ymm")
        s_y = sem("s_y")
        s_out = sem("s_out")

        block = ctx.enter_context(nc.Block())

        @block.sync
        def _(sp):
            sp.dma_start(idx[:], ids.rearrange("(t p) f -> p t f", p=P)).then_inc(s_idx, 16)
            sp.dma_start(emb[:, :, 0, :], bottom.rearrange("(t p) d -> p t d", p=P)).then_inc(s_bottom, 16)
            sp.dma_start(w1p[:], w1_pairs).then_inc(s_w1, 16)
            sp.dma_start(w1b[:], w1_bottom).then_inc(s_w1, 16)
            sp.dma_start(b1s[:], b1).then_inc(s_w1, 16)
            sp.dma_start(w2s[:], w2.rearrange("(k p) n -> p k n", p=P)).then_inc(s_w2, 16)
            sp.dma_start(b2s[:], b2).then_inc(s_w2, 16)
            sp.dma_start(w3s[:], w3).then_inc(s_w2, 16)
            sp.wait_ge(s_y, TILES)
            sp.dma_start(out.rearrange("b o -> o b"), y[:]).then_inc(s_out, 16)
            sp.wait_ge(s_out, 16)

        @block.gpsimd
        def _(pool):
            nc.gpsimd.memset(ident[:], 0.0).then_inc(s_ident0, 1)
            pool.wait_ge(s_ident0, 1)
            nc.gpsimd.affine_select(out=ident[:], in_=ident[:], compare_op=ALU.not_equal, fill=1.0, base=0,
                                    pattern=[[-1, P]], channel_multiplier=1).then_inc(s_ident, 1)
            pool.wait_ge(s_idx, 16)
            for t in range(TILES):
                for q in range(QUADS):
                    for slot in quad_slots(q):
                        if slot:
                            f = slot - 1
                            pool.indirect_dma_start(
                                emb[:, t, slot, :], None, tables[f],
                                bass.IndirectOffsetOnAxis(ap=idx[:, t, f:f + 1], axis=0),
                            ).then_inc(s_gather[t][q], 16)

        def quad_number(t, q):
            return t * QUADS + q

        def wait_embT(eng, t, q):
            n = quad_number(t, q)
            eng.wait_ge(s_trD, n // 2 + 1)
            if n:
                eng.wait_ge(s_trA, (n + 1) // 2)

        @block.tensor
        def _(pe):
            def transposes(t, q):
                n = quad_number(t, q)
                if n >= 2:
                    pe.wait_ge(s_trA if n % 2 else s_trD, n // 2)
                if q == 0 and t == 0:
                    pe.wait_ge(s_bottom, 16)
                pe.wait_ge(s_gather[t][q], 16 * sum(1 for s in quad_slots(q) if s))
                for k, slot in enumerate(quad_slots(q)):
                    last = nc.tensor.transpose(tr_ps[:, n % 2, k, :], emb[:, t, slot, :], ident[:])
                last.then_inc(s_tr, 1)

            def gram(t, h):
                g = 2 * t + h
                if h == 0:
                    wait_embT(pe, t, QUADS - 1)
                if g:
                    pe.wait_ge(s_pairD, g)
                    pe.wait_ge(s_pairA, g)
                for m in range(NMM):
                    b0 = t * P + h * HALF + m * PACK
                    last = nc.tensor.matmul(gram_ps[:, m, 0:PACK * PAIR_COLS],
                                            embT[:, b0:b0 + PACK, :].rearrange("p b s -> p (b s)"),
                                            embT[:, b0:b0 + PACK, 1:NF], start=True, stop=True)
                last.then_inc(s_gram, 1)

            def layer1(t):
                pe.wait_ge(s_pairD, 2 * t + 2)
                pe.wait_ge(s_pairA, 2 * t + 2)
                if t:
                    pe.wait_ge(s_h1, N1 * t)
                bs = slice(t * P, (t + 1) * P)
                for n in range(N1):
                    ns = slice(n * P, (n + 1) * P)
                    nc.tensor.matmul(h1_ps[:, n, :], w1b[:, ns], embT[:, bs, 0], start=True, stop=False)
                    for g in range(KG):
                        rows = min(4, PAIR_COLS - 4 * g) * SLOT
                        last = nc.tensor.matmul(h1_ps[:, n, :], w1p[0:rows, g, ns], pairs[0:rows, g, bs],
                                                start=False, stop=(g == KG - 1))
                last.then_inc(s_h1mm, 1)

            def layer2(t):
                pe.wait_ge(s_h1, N1 * (t + 1))
                if t:
                    pe.wait_ge(s_h2, N2 * t)
                    pe.wait_ge(s_y, t)
                for n in range(N2):
                    for k in range(N1):
                        last = nc.tensor.matmul(h2_ps[:, n, :], w2s[:, k, n * P:(n + 1) * P], h1[:, t, k, :],
                                                start=(k == 0), stop=(k == N1 - 1))
                last.then_inc(s_h2mm, 1)

            def layer3(t):
                pe.wait_ge(s_h2, N2 * (t + 1))
                for k in range(N2):
                    last = nc.tensor.matmul(h2_ps[0:1, 2, :], w3s[:, k:k + 1], h2[:, t, k, :],
                                            start=(k == 0), stop=(k == N2 - 1))
                last.then_inc(s_ymm, 1)

            pe.wait_ge(s_ident, 1)
            for t in range(TILES + 1):
                for q in range(QUADS):
                    if t:
                        if q == 0:
                            if t == 1:
                                pe.wait_ge(s_pad, 1)
                            gram(t - 1, 0)
                        if q == 1:
                            gram(t - 1, 1)
                        if q == 2:
                            if t == 1:
                                pe.wait_ge(s_w1, 48)
                            layer1(t - 1)
                        if q == 3:
                            if t == 1:
                                pe.wait_ge(s_w2, 48)
                            layer2(t - 1)
                        if q == 4:
                            layer3(t - 1)
                    if t < TILES:
                        transposes(t, q)

        def move_quad(copy, t, q, done):
            n = quad_number(t, q)
            w = len(quad_slots(q))
            copy(embT[:, t * P:(t + 1) * P, 4 * q:4 * q + w].rearrange("p b s -> p s b"),
                 tr_ps[:, n % 2, 0:w, :]).then_inc(done, 1)

        def move_pairs(copy, t, h, samples, done):
            b0 = t * P + h * HALF
            for s in samples:
                for jj in range(4):
                    gs = len(range(jj, PAIR_COLS, 4))
                    src = gram_ps[s * SLOT:(s + 1) * SLOT, :, s * PAIR_COLS + jj:(s + 1) * PAIR_COLS:4]
                    dst = pairs[jj * SLOT:(jj + 1) * SLOT, 0:gs, b0 + s:b0 + HALF:PACK]
                    last = copy(dst.rearrange("p g m -> p m g"), src)
            last.then_inc(done, 1)

        @block.vector
        def _(dve):
            nc.vector.memset(embT[:, :, NF:SLOT], 0.0).then_inc(s_pad, 1)
            for t in range(TILES + 1):
                for q in range(QUADS):
                    if t and q < 2:
                        dve.wait_ge(s_gram, 2 * (t - 1) + q + 1)
                        move_pairs(nc.vector.tensor_copy, t - 1, q, (0, 1), s_pairD)
                    if t < TILES and quad_number(t, q) % 2 == 0:
                        dve.wait_ge(s_tr, quad_number(t, q) + 1)
                        move_quad(nc.vector.tensor_copy, t, q, s_trD)

        @block.scalar
        def _(act):
            for t in range(TILES + 1):
                for q in range(QUADS):
                    if t and q < 2:
                        act.wait_ge(s_gram, 2 * (t - 1) + q + 1)
                        move_pairs(nc.scalar.copy, t - 1, q, (2, 3), s_pairA)
                    if t and q == 2:
                        act.wait_ge(s_h1mm, t)
                        for n in range(N1):
                            nc.scalar.activation(h1[:, t - 1, n, :], h1_ps[:, n, :], ACT.Relu,
                                                 bias=b1s[:, n:n + 1]).then_inc(s_h1, 1)
                    if t and q == 3:
                        act.wait_ge(s_h2mm, t)
                        for n in range(N2):
                            nc.scalar.activation(h2[:, t - 1, n, :], h2_ps[:, n, :], ACT.Relu,
                                                 bias=b2s[:, n:n + 1]).then_inc(s_h2, 1)
                    if t and q == 4:
                        act.wait_ge(s_ymm, t)
                        nc.scalar.copy(y[:, (t - 1) * P:t * P], h2_ps[0:1, 2, :]).then_inc(s_y, 1)
                    if t < TILES and quad_number(t, q) % 2 == 1:
                        act.wait_ge(s_tr, quad_number(t, q) + 1)
                        move_quad(nc.scalar.copy, t, q, s_trA)


def kernel(**inputs):
    import numpy as np
    import concourse.bacc as bacc
    from concourse.bass_utils import run_bass_kernel_spmd

    npairs = NF * (NF - 1) // 2
    w1 = np.asarray(inputs["W_top1"])
    i, j = np.triu_indices(NF, k=1)
    w1_pairs = np.zeros((P, KG, H1), w1.dtype)
    w1_pairs[SLOT * ((j - 1) % 4) + i, (j - 1) // 4] = w1[:npairs]
    laid = {
        "bottom": inputs["r_bottom_output"],
        "ids": inputs["ids"],
        "w1_pairs": w1_pairs,
        "w1_bottom": w1[npairs:],
        "b1": np.asarray(inputs["b_top1"]).reshape(N1, P).T,
        "w2": inputs["W_top2"],
        "b2": np.asarray(inputs["b_top2"]).reshape(N2, P).T,
        "w3": np.asarray(inputs["W_top3"]).reshape(N2, P).T,
    }
    for f in range(NTAB):
        laid[f"tbl_{f}"] = inputs[f"tbl_{f}"]

    nc = bacc.Bacc("TRN2", target_bir_lowering=False, num_devices=1)
    arrays, aps = {}, {}
    for name, a in laid.items():
        a = np.ascontiguousarray(a)
        arrays[f"in_{name}"] = a
        aps[name] = nc.dram_tensor(f"in_{name}", a.shape, mybir.dt.from_np(a.dtype), kind="ExternalInput").ap()
    out = nc.dram_tensor("out_y", (B, 1), F32, kind="ExternalOutput").ap()
    build(nc, aps["bottom"], aps["ids"], [aps[f"tbl_{f}"] for f in range(NTAB)], aps["w1_pairs"], aps["w1_bottom"],
          aps["b1"], aps["w2"], aps["b2"], aps["w3"], out)
    r = run_bass_kernel_spmd(nc, [arrays], core_ids=[0])
    return r.results[0]["out_y"]
```

```python
from contextlib import ExitStack

import concourse.bass as bass
from concourse import mybir

F32 = mybir.dt.float32
F32R = mybir.dt.float32r
BF16 = mybir.dt.bfloat16
I32 = mybir.dt.int32
ALU = mybir.AluOpType
ACT = mybir.ActivationFunctionType

P = 128
B = 512
D = 128
TILES = B // P
LAST = TILES - 1
VOCAB = [12500, 125000, 1000, 1250, 12500, 12500, 1000, 1000, 1000, 1250, 1250, 12500, 12500, 1000, 12500, 1250, 12500,
         12500, 12500, 1000, 1000, 1000, 1000, 1000, 1000, 1000]
NTAB = len(VOCAB)
NF = NTAB + 1
PAIRS = NF * (NF - 1) // 2

CHUNKS = 8
TROWS = 1000
TP = TROWS // CHUNKS
ONEHOT = 7
RAWS = 3
WARM = 16
ONEHOT_TABLES = [f for f in range(NTAB) if VOCAB[f] == TROWS][:ONEHOT]
GATHER_TABLES = [f for f in range(NTAB) if f not in ONEHOT_TABLES]
SLOT_TABLE = [None] + ONEHOT_TABLES + GATHER_TABLES
GATHERED = len(GATHER_TABLES)
FIRST_GATHERED = 1 + ONEHOT
QUADS = (GATHERED + 3) // 4

SLOT = 32
PACK = P // SLOT
GROUP = 32
PRODUCTS = GROUP // PACK
GROUPS = P // GROUP
THIRD = NF // 3
PAIR_CHUNKS = (THIRD + 1) // 2
CHUNK_ROWS = [P] * (PAIR_CHUNKS - 1) + [3 * SLOT]
H1, H2 = 512, 256
N1, N2 = H1 // P, H2 // P

def quad_slots(q):
    first = FIRST_GATHERED + 4 * q
    return range(first, min(first + 4, NF))


def pair_place(a, b):
    low, high = a // THIRD, b // THIRD
    row, k = (b, a % THIRD) if (low, high) == (0, 2) else (a, b % THIRD)
    second = (low, high) in ((0, 1), (1, 1), (0, 2))
    return 2 * second + k % 2, k // 2, row


def plan():
    steps = [("bottom", 0, 0)]
    for i in range(max(ONEHOT, QUADS)):
        if i < ONEHOT:
            steps.append(("onehot", 0, i))
        if i < QUADS:
            steps.append(("quad", 0, i))
    for t in range(1, TILES):
        quads = [("quad", t, q) for q in range(QUADS)]
        grams = [("gram", t - 1, g) for g in range(GROUPS)]
        before = t >= 2
        steps += grams[0:2] + quads[0:1] + grams[2:3] + [("layer2", t - 2, 0)] * before + grams[3:4]
        steps += quads[1:2] + [("layer3", t - 2, 0)] * before + quads[2:-1]
        steps += [("layer1", t - 1, 0), quads[-1]] if t == LAST else [quads[-1], ("layer1", t - 1, 0)]
    grams = [("gram", LAST, g) for g in range(GROUPS)]
    return steps + grams[0:2] + [("layer2", LAST - 1, 0)] + grams[2:4] + [("layer3", LAST - 1, 0)] + [
        ("last_layer1", LAST, 0), ("last_layer2", LAST, 0), ("last_layer3", LAST, 0)]


STEPS = plan()
TURNS = [s for s in STEPS if s[0] in ("bottom", "onehot", "quad")]
TURN_BANKS, GRAM_BANKS = 2, 4
BANK = [n % (TURN_BANKS + GRAM_BANKS if t == 0 else TURN_BANKS) for n, (step, t, i) in enumerate(TURNS)]
BEFORE = [max((m for m in range(n) if BANK[m] == BANK[n]), default=None) for n in range(len(TURNS))]
BY_DVE = [t > 0 and n % 2 == 0 for n, (step, t, i) in enumerate(TURNS)]


def turn(step, t, i):
    return TURNS.index((step, t, i))


def last_turn(t):
    return max(n for n, (step, u, q) in enumerate(TURNS) if u == t)


def build(nc, bottom, ids, ids_onehot, tables, w1_pairs, w1_bottom, b1, w2, b2, w3, out):
    ctx = ExitStack()
    with ctx:
        def sb(name, shape, dt=F32):
            return ctx.enter_context(nc.sbuf_tensor(name, shape, dt))

        def ps(name, shape, dt=F32):
            return ctx.enter_context(nc.psum_tensor(name, shape, dt))

        def sem(name):
            return ctx.enter_context(nc.semaphore(name))

        idx = sb("idx", [P, TILES, NTAB], I32)
        idb = sb("idb", [TP, RAWS, 2, B], I32)
        rowid = sb("rowid", [TP, CHUNKS // 2])
        raw = sb("raw", [TP, RAWS, CHUNKS, D])
        hi = sb("hi", [TP, 2, CHUNKS, D], F32R)
        lo = sb("lo", [TP, 2, CHUNKS, D], F32R)
        pick = sb("pick", [TP, CHUNKS // 2, 2, B], F32R)
        bot = sb("bot", [P, TILES, D])
        emb = sb("emb", [P, 2, GATHERED, D])
        embT = sb("embT", [P, B, SLOT])
        pairs = sb("pairs", [P, PAIR_CHUNKS, B])
        w1p = sb("w1p", [P, PAIR_CHUNKS, H1])
        w1b = sb("w1b", [P, H1])
        w2s = sb("w2s", [P, N1, H2])
        w3s = sb("w3s", [P, N2])
        b1s = sb("b1s", [P, N1])
        b2s = sb("b2s", [P, N2])
        h1 = sb("h1", [P, 2, N1, P])
        h2 = sb("h2", [P, 2, N2, P])
        y = sb("y", [1, B])
        ident = sb("ident", [P, P])
        scratch = sb("scratch", [P, 1])
        zeros = sb("zeros", [P, B], BF16)

        work_ps = ps("work_ps", [P, TURN_BANKS + GRAM_BANKS, 4, P])
        gram_ps = work_ps[:, TURN_BANKS:, :, :].rearrange("p b m w -> p (b m) w")
        h1_ps = ps("h1_ps", [P, N1, P])
        h2_ps = ps("h2_ps", [P, 4, P])

        s_idx = sem("s_idx")
        s_idb = [sem(f"s_idb_{k}") for k in range(ONEHOT)]
        s_bottom = sem("s_bottom")
        s_raw = [sem(f"s_raw_{b}") for b in range(RAWS)]
        s_w1 = sem("s_w1")
        s_w2 = sem("s_w2")
        s_gather = [[sem(f"s_gather_{t}_{q}") for q in range(QUADS)] for t in range(TILES)]
        s_zeros = sem("s_zeros")
        s_ident0 = sem("s_ident0")
        s_ident = sem("s_ident")
        s_rowid = sem("s_rowid")
        s_pad = sem("s_pad")
        s_less = sem("s_less")
        s_hi = sem("s_hi")
        s_lo = sem("s_lo")
        s_pick = sem("s_pick")
        s_picked = sem("s_picked")
        s_turn = sem("s_turn")
        s_turnD = sem("s_turnD")
        s_turnA = sem("s_turnA")
        s_gram = sem("s_gram")
        s_wholeD = sem("s_wholeD")
        s_wholeA = sem("s_wholeA")
        s_pairD = sem("s_pairD")
        s_pairA = sem("s_pairA")
        s_h1mm = sem("s_h1mm")
        s_h1 = sem("s_h1")
        s_h2mm = sem("s_h2mm")
        s_h2 = sem("s_h2")
        s_ymm = sem("s_ymm")
        s_y = sem("s_y")
        s_last1mm = sem("s_last1mm")
        s_last1D = sem("s_last1D")
        s_last1A = sem("s_last1A")
        s_last2mm = sem("s_last2mm")
        s_last2D = sem("s_last2D")
        s_last2A = sem("s_last2A")
        s_out = sem("s_out")

        block = ctx.enter_context(nc.Block())

        def load_table(eng, k):
            f = ONEHOT_TABLES[k]
            src = tables[f].rearrange("(p c) d -> p c d", c=CHUNKS)
            whole = TP // 16 * 16
            eng.dma_start(raw[0:whole, k % RAWS], src[0:whole]).then_inc(s_raw[k % RAWS], 16)
            eng.dma_start(raw[whole:TP, k % RAWS], src[whole:TP]).then_inc(s_raw[k % RAWS], 16)

        def load_ids(eng, k):
            eng.dma_start(idb[:, k % RAWS, 0, :], ids_onehot[k].partition_broadcast(TP)).then_inc(s_idb[k], 16)

        @block.sync
        def _(sp):
            sp.dma_start(idx[:], ids.rearrange("(t p) f -> p t f", p=P)).then_inc(s_idx, 16)
            load_table(sp, 0)
            sp.dma_start(bot[:], bottom.rearrange("(t p) d -> p t d", p=P)).then_inc(s_bottom, 16)
            for k in range(1, ONEHOT):
                if k >= RAWS:
                    sp.wait_ge(s_pick, (k - RAWS + 1) * CHUNKS // 2)
                load_ids(sp, k)
                if k >= RAWS:
                    sp.wait_ge(s_lo, k - RAWS + 1)
                load_table(sp, k)
            sp.wait_ge(s_turn, turn("onehot", 0, ONEHOT - 1))
            sp.dma_start(w1p[:], w1_pairs).then_inc(s_w1, 16)
            sp.dma_start(w1b[:], w1_bottom).then_inc(s_w1, 16)
            sp.dma_start(b1s[:], b1).then_inc(s_w1, 16)
            sp.dma_start(w2s[:], w2.rearrange("(k p) n -> p k n", p=P)).then_inc(s_w2, 16)
            sp.dma_start(b2s[:], b2).then_inc(s_w2, 16)
            sp.dma_start(w3s[:], w3).then_inc(s_w2, 16)
            sp.wait_ge(s_y, TILES)
            sp.dma_start(out.rearrange("b o -> o b"), y[:]).then_inc(s_out, 16)
            sp.wait_ge(s_out, 16)

        @block.gpsimd
        def _(pool):
            nc.gpsimd.memset(ident[:], 0.0).then_inc(s_ident0, 1)
            nc.gpsimd.iota(rowid[:], [[1, CHUNKS // 2]], base=0, channel_multiplier=CHUNKS,
                           allow_small_or_imprecise_dtypes=True).then_inc(s_rowid, 1)
            pool.wait_ge(s_ident0, 1)
            nc.gpsimd.affine_select(out=ident[:], in_=ident[:], compare_op=ALU.not_equal, fill=1.0, base=0,
                                    pattern=[[-1, P]], channel_multiplier=1).then_inc(s_ident, 1)
            pool.wait_ge(s_idx, 16)
            for t in range(TILES):
                for q in range(QUADS):
                    if t >= 2:
                        pool.wait_ge(s_turn, turn("quad", t - 2, q) + 1)
                    for slot in quad_slots(q):
                        f = SLOT_TABLE[slot]
                        pool.indirect_dma_start(
                            emb[:, t % 2, slot - FIRST_GATHERED, :], None, tables[f],
                            bass.IndirectOffsetOnAxis(ap=idx[:, t, f:f + 1], axis=0),
                        ).then_inc(s_gather[t][q], 16)

        def wait_emptied(eng, n):
            eng.wait_ge(s_turnD if BY_DVE[n] else s_turnA, BY_DVE[:n + 1].count(BY_DVE[n]))

        def wait_turns(eng, n):
            if True in BY_DVE[:n + 1]:
                eng.wait_ge(s_turnD, BY_DVE[:n + 1].count(True))
            eng.wait_ge(s_turnA, BY_DVE[:n + 1].count(False))

        @block.tensor
        def _(pe):
            def bank_free(n):
                if BEFORE[n] is not None:
                    wait_emptied(pe, BEFORE[n])

            def turn_bottom(n):
                bank_free(n)
                pe.wait_ge(s_ident, 1)
                pe.wait_ge(s_bottom, 16)
                for t in range(TILES):
                    last = nc.tensor.transpose(work_ps[:, BANK[n], t, :], bot[:, t, :], ident[:])
                last.then_inc(s_turn, 1)

            def turn_quad(n, t, q):
                bank_free(n)
                slots = quad_slots(q)
                pe.wait_ge(s_gather[t][q], 16 * len(slots))
                for k, slot in enumerate(slots):
                    last = nc.tensor.transpose(work_ps[:, BANK[n], k, :], emb[:, t % 2, slot - FIRST_GATHERED, :], ident[:])
                last.then_inc(s_turn, 1)

            def onehot(n, k):
                bank_free(n)
                pe.wait_ge(s_hi, k + 1)
                pe.wait_ge(s_lo, k + 1)
                acc = work_ps[:, BANK[n], :, :].rearrange("p t b -> p (t b)")
                for c in range(CHUNKS // 2):
                    pe.wait_ge(s_pick, k * CHUNKS // 2 + c + 1)
                    for half in range(2):
                        chunk = c + half * CHUNKS // 2
                        nc.tensor.matmul(acc, hi[:, k % 2, chunk, :], pick[:, c, half, :],
                                         start=(c + half == 0), stop=False)
                        last = nc.tensor.matmul(acc, lo[:, k % 2, chunk, :], pick[:, c, half, :],
                                                start=False, stop=(chunk == CHUNKS - 1))
                    if c < CHUNKS // 2 - 1:
                        last.then_inc(s_picked, 1)
                last.then_inc(s_turn, 1)

            def gram(t, h):
                g = GROUPS * t + h
                if h == 0:
                    wait_turns(pe, last_turn(t))
                if g == 0:
                    pe.wait_ge(s_pad, 1)
                if g >= 2:
                    pe.wait_ge(s_pairD, g - 1)
                    pe.wait_ge(s_pairA, g - 1)
                for m in range(PRODUCTS):
                    b0 = t * P + h * GROUP + m * PACK
                    last = nc.tensor.matmul(gram_ps[:, g % 2 * PRODUCTS + m, 0:PACK * NF],
                                            embT[:, b0:b0 + PACK, :].rearrange("p b s -> p (b s)"),
                                            embT[:, b0:b0 + PACK, 0:NF], start=True, stop=True)
                last.then_inc(s_gram, 1)

            def layer1_part(acc, t, n):
                bs = slice(t * P, (t + 1) * P)
                ns = slice(n * P, (n + 1) * P)
                nc.tensor.matmul(acc, w1b[:, ns], embT[:, bs, 0], start=True, stop=False)
                for g, rows in enumerate(CHUNK_ROWS):
                    last = nc.tensor.matmul(acc, w1p[0:rows, g, ns], pairs[0:rows, g, bs],
                                            start=False, stop=(g == PAIR_CHUNKS - 1))
                return last

            def layer1(t):
                if t == 0:
                    pe.wait_ge(s_w1, 48)
                pe.wait_ge(s_pairD, GROUPS * (t + 1))
                pe.wait_ge(s_pairA, GROUPS * (t + 1))
                if t:
                    pe.wait_ge(s_h1, N1 * t)
                for n in range(N1):
                    last = layer1_part(h1_ps[:, n, :], t, n)
                last.then_inc(s_h1mm, 1)

            def layer2(t):
                if t == 0:
                    pe.wait_ge(s_w2, 48)
                pe.wait_ge(s_h1, N1 * (t + 1))
                if t:
                    pe.wait_ge(s_h2, N2 * t)
                    pe.wait_ge(s_y, t)
                for n in range(N2):
                    for k in range(N1):
                        last = nc.tensor.matmul(h2_ps[:, n, :], w2s[:, k, n * P:(n + 1) * P], h1[:, t % 2, k, :],
                                                start=(k == 0), stop=(k == N1 - 1))
                last.then_inc(s_h2mm, 1)

            def layer3(t):
                pe.wait_ge(s_h2, N2 * (t + 1))
                for k in range(N2):
                    last = nc.tensor.matmul(h2_ps[0:1, N2, :], w3s[:, k:k + 1], h2[:, t % 2, k, :],
                                            start=(k == 0), stop=(k == N2 - 1))
                last.then_inc(s_ymm, 1)

            last1 = [gram_ps[:, 4 * n, :] for n in range(N1)]
            last2 = [h2_ps[:, 0, :], h1_ps[:, 0, :]]

            pe.wait_ge(s_zeros, 1)
            for _ in range(WARM):
                nc.tensor.matmul(h1_ps[:, :, :].rearrange("p n b -> p (n b)"), zeros[:, 0:P], zeros[:], start=True, stop=True)

            for step, t, i in STEPS:
                if step == "bottom":
                    turn_bottom(turn(step, t, i))
                if step == "onehot":
                    onehot(turn(step, t, i), i)
                if step == "quad":
                    turn_quad(turn(step, t, i), t, i)
                if step == "gram":
                    gram(t, i)
                if step == "layer1":
                    layer1(t)
                if step == "layer2":
                    layer2(t)
                if step == "layer3":
                    layer3(t)
                if step == "last_layer1":
                    pe.wait_ge(s_pairD, GROUPS * TILES)
                    pe.wait_ge(s_pairA, GROUPS * TILES)
                    for n in range(N1):
                        layer1_part(last1[n], t, n).then_inc(s_last1mm, 1)
                if step == "last_layer2":
                    pe.wait_ge(s_h2, N2 * LAST)
                    pe.wait_ge(s_y, LAST)
                    for k in range(N1):
                        pe.wait_ge(s_last1A if k % 2 else s_last1D, k // 2 + 1)
                        for n in range(N2):
                            last = nc.tensor.matmul(last2[n], w2s[:, k, n * P:(n + 1) * P], h1[:, t % 2, k, :],
                                                    start=(k == 0), stop=(k == N1 - 1))
                            if k == N1 - 1:
                                last.then_inc(s_last2mm, 1)
                if step == "last_layer3":
                    for k in range(N2):
                        pe.wait_ge(s_last2A if k % 2 else s_last2D, 1)
                        last = nc.tensor.matmul(gram_ps[0:1, 0, :], w3s[:, k:k + 1], h2[:, t % 2, k, :],
                                                start=(k == 0), stop=(k == N2 - 1))
                    last.then_inc(s_ymm, 1)

        def move_turned(copy, n, step, t, i, done):
            if step == "bottom":
                src, dst = work_ps[:, BANK[n], :, :].rearrange("p t b -> p (t b)"), embT[:, :, 0]
            elif step == "onehot":
                src, dst = work_ps[:, BANK[n], :, :].rearrange("p t b -> p (t b)"), embT[:, :, 1 + i]
            else:
                slots = quad_slots(i)
                src = work_ps[:, BANK[n], 0:len(slots), :]
                dst = embT[:, t * P:(t + 1) * P, slots[0]:slots[-1] + 1].rearrange("p b s -> p s b")
            copy(dst, src).then_inc(done, 1)

        def move_pairs(copy, t, h, samples, third_of, rows):
            b0 = t * P + h * GROUP
            first = (GROUPS * t + h) % 2 * PRODUCTS
            for s in samples:
                for quadrant in range(4):
                    half, odd = divmod(quadrant, 2)
                    chunks = len(range(odd, THIRD, 2))
                    at = s * NF + third_of[half] * THIRD + odd
                    src = gram_ps[s * SLOT:s * SLOT + rows[half], first:first + PRODUCTS, at:at + 2 * chunks - 1:2]
                    dst = pairs[quadrant * SLOT:quadrant * SLOT + rows[half], 0:chunks, b0 + s:b0 + GROUP:PACK]
                    last = copy(dst.rearrange("p g m -> p m g"), src)
            return last

        @block.vector
        def _(dve):
            def one_hot(k, first, end):
                dve.wait_ge(s_less, k + 1)
                for c in range(first, end):
                    if k:
                        if c < CHUNKS // 2 - 1:
                            dve.wait_ge(s_picked, (k - 1) * (CHUNKS // 2 - 1) + c + 1)
                        else:
                            dve.wait_ge(s_turn, turn("onehot", 0, k - 1) + 1)
                    nc.vector.tensor_scalar(pick[:, c], idb[:, k % RAWS], rowid[:, c:c + 1], None,
                                            ALU.is_equal).then_inc(s_pick, 1)

            def low_parts(k):
                dve.wait_ge(s_hi, k + 1)
                nc.vector.tensor_tensor(lo[:, k % 2], raw[:, k % RAWS], hi[:, k % 2], ALU.subtract).then_inc(s_lo, 1)

            nc.vector.memset(zeros[:], 0.0).then_inc(s_zeros, 1)
            nc.vector.memset(embT[:, :, NF:SLOT], 0.0)
            nc.vector.memset(pairs[SLOT:2 * SLOT, PAIR_CHUNKS - 1, :], 0.0).then_inc(s_pad, 1)
            dve.wait_ge(s_rowid, 1)
            one_hot(0, 0, 2)
            low_parts(0)
            one_hot(0, 2, CHUNKS // 2)
            for step, t, i in STEPS:
                if step == "onehot" and i + 1 < ONEHOT:
                    low_parts(i + 1)
                    one_hot(i + 1, 0, CHUNKS // 2)
                if step in ("bottom", "onehot", "quad"):
                    n = turn(step, t, i)
                    if BY_DVE[n]:
                        dve.wait_ge(s_turn, n + 1)
                        move_turned(nc.vector.tensor_copy, n, step, t, i, s_turnD)
                if step == "gram":
                    dve.wait_ge(s_gram, GROUPS * t + i + 1)
                    move_pairs(nc.vector.tensor_copy, t, i, (0, 1), (2, 0), (SLOT, SLOT)).then_inc(s_wholeD, 1)
                    dve.wait_ge(s_wholeD, GROUPS * t + i + 1)
                    move_pairs(nc.vector.tensor_copy, t, i, (0, 1), (0, 1), (THIRD, 2 * THIRD)).then_inc(s_pairD, 1)
                if step == "last_layer1":
                    for n in range(0, N1, 2):
                        dve.wait_ge(s_last1mm, n + 1)
                        nc.vector.tensor_scalar(h1[:, t % 2, n, :], gram_ps[:, 4 * n, :], b1s[:, n:n + 1], 0.0,
                                                ALU.add, ALU.max).then_inc(s_last1D, 1)
                if step == "last_layer2":
                    dve.wait_ge(s_last2mm, 1)
                    nc.vector.tensor_scalar(h2[:, t % 2, 0, :], h2_ps[:, 0, :], b2s[:, 0:1], 0.0,
                                            ALU.add, ALU.max).then_inc(s_last2D, 1)
                if step == "last_layer3":
                    dve.wait_ge(s_ymm, TILES)
                    nc.vector.tensor_copy(y[:, t * P:(t + 1) * P], gram_ps[0:1, 0, :]).then_inc(s_y, 1)

        @block.scalar
        def _(act):
            load_ids(act, 0)
            act.wait_ge(s_zeros, 1)
            nc.scalar.copy(scratch[:], zeros[:, 0:1])

            def less(k):
                act.wait_ge(s_idb[k], 16)
                if k >= RAWS:
                    act.wait_ge(s_pick, (k - RAWS + 1) * CHUNKS // 2)
                nc.scalar.activation(idb[:, k % RAWS, 1, :], idb[:, k % RAWS, 0, :], ACT.Copy,
                                     bias=-float(CHUNKS // 2)).then_inc(s_less, 1)

            def high_parts(k):
                if k >= 2:
                    act.wait_ge(s_turn, turn("onehot", 0, k - 2) + 1)
                act.wait_ge(s_raw[k % RAWS], 32 * (k // RAWS + 1))
                nc.scalar.copy(hi[:, k % 2], raw[:, k % RAWS]).then_inc(s_hi, 1)

            less(0)
            high_parts(0)
            for step, t, i in STEPS:
                if step == "onehot" and i + 1 < ONEHOT:
                    less(i + 1)
                    high_parts(i + 1)
                if step in ("bottom", "onehot", "quad"):
                    n = turn(step, t, i)
                    if not BY_DVE[n]:
                        act.wait_ge(s_turn, n + 1)
                        move_turned(nc.scalar.copy, n, step, t, i, s_turnA)
                if step == "gram":
                    act.wait_ge(s_gram, GROUPS * t + i + 1)
                    move_pairs(nc.scalar.copy, t, i, (2, 3), (2, 0), (SLOT, SLOT)).then_inc(s_wholeA, 1)
                    act.wait_ge(s_wholeA, GROUPS * t + i + 1)
                    move_pairs(nc.scalar.copy, t, i, (2, 3), (0, 1), (THIRD, 2 * THIRD)).then_inc(s_pairA, 1)
                if step == "layer1":
                    act.wait_ge(s_h1mm, t + 1)
                    for n in range(N1):
                        nc.scalar.activation(h1[:, t % 2, n, :], h1_ps[:, n, :], ACT.Relu,
                                             bias=b1s[:, n:n + 1]).then_inc(s_h1, 1)
                if step == "layer2":
                    act.wait_ge(s_h2mm, t + 1)
                    for n in range(N2):
                        nc.scalar.activation(h2[:, t % 2, n, :], h2_ps[:, n, :], ACT.Relu,
                                             bias=b2s[:, n:n + 1]).then_inc(s_h2, 1)
                if step == "layer3":
                    act.wait_ge(s_ymm, t + 1)
                    nc.scalar.copy(y[:, t * P:(t + 1) * P], h2_ps[0:1, N2, :]).then_inc(s_y, 1)
                if step == "last_layer1":
                    for n in range(1, N1, 2):
                        act.wait_ge(s_last1mm, n + 1)
                        nc.scalar.activation(h1[:, t % 2, n, :], gram_ps[:, 4 * n, :], ACT.Relu,
                                             bias=b1s[:, n:n + 1]).then_inc(s_last1A, 1)
                if step == "last_layer2":
                    act.wait_ge(s_last2mm, 2)
                    nc.scalar.activation(h2[:, t % 2, 1, :], h1_ps[:, 0, :], ACT.Relu,
                                         bias=b2s[:, 1:2]).then_inc(s_last2A, 1)


def kernel(**inputs):
    import numpy as np
    import concourse.bacc as bacc
    from concourse.bass_utils import run_bass_kernel_spmd

    feature = [0] + [f + 1 for f in SLOT_TABLE[1:]]
    w1 = np.asarray(inputs["W_top1"])
    w1_pairs = np.zeros((P, PAIR_CHUNKS, H1), w1.dtype)
    for b in range(NF):
        for a in range(b):
            low, high = sorted((feature[a], feature[b]))
            quadrant, chunk, row = pair_place(a, b)
            w1_pairs[SLOT * quadrant + row, chunk] = w1[low * NF - low * (low + 1) // 2 + high - low - 1]
    laid = {
        "bottom": inputs["r_bottom_output"],
        "ids": inputs["ids"],
        "ids_onehot": np.asarray(inputs["ids"])[:, ONEHOT_TABLES].T,
        "w1_pairs": w1_pairs,
        "w1_bottom": w1[PAIRS:],
        "b1": np.asarray(inputs["b_top1"]).reshape(N1, P).T,
        "w2": inputs["W_top2"],
        "b2": np.asarray(inputs["b_top2"]).reshape(N2, P).T,
        "w3": np.asarray(inputs["W_top3"]).reshape(N2, P).T,
    }
    for f in range(NTAB):
        laid[f"tbl_{f}"] = inputs[f"tbl_{f}"]

    nc = bacc.Bacc("TRN2", target_bir_lowering=False, num_devices=1)
    arrays, aps = {}, {}
    for name, a in laid.items():
        a = np.ascontiguousarray(a)
        arrays[f"in_{name}"] = a
        aps[name] = nc.dram_tensor(f"in_{name}", a.shape, mybir.dt.from_np(a.dtype), kind="ExternalInput").ap()
    out = nc.dram_tensor("out_y", (B, 1), F32, kind="ExternalOutput").ap()
    build(nc, aps["bottom"], aps["ids"], aps["ids_onehot"], [aps[f"tbl_{f}"] for f in range(NTAB)], aps["w1_pairs"],
          aps["w1_bottom"], aps["b1"], aps["w2"], aps["b2"], aps["w3"], out)
    r = run_bass_kernel_spmd(nc, [arrays], core_ids=[0])
    return r.results[0]["out_y"]
```

```python
from contextlib import ExitStack

import concourse.bass as bass
from concourse import mybir

F32 = mybir.dt.float32
F32R = mybir.dt.float32r
BF16 = mybir.dt.bfloat16
I32 = mybir.dt.int32
ALU = mybir.AluOpType
ACT = mybir.ActivationFunctionType

P = 128
B = 512
D = 128
TILES = B // P
LAST = TILES - 1
VOCAB = [12500, 125000, 1000, 1250, 12500, 12500, 1000, 1000, 1000, 1250, 1250, 12500, 12500, 1000, 12500, 1250, 12500,
         12500, 12500, 1000, 1000, 1000, 1000, 1000, 1000, 1000]
NTAB = len(VOCAB)
NF = NTAB + 1
PAIRS = NF * (NF - 1) // 2

CHUNKS = 8
TROWS = 1000
TP = TROWS // CHUNKS
ONEHOT = 8
RAWS = 3
SPLITS = 3
AHEAD = 2
WARM = 13
ONEHOT_TABLES = [f for f in range(NTAB) if VOCAB[f] == TROWS][:ONEHOT]
GATHER_TABLES = [f for f in range(NTAB) if f not in ONEHOT_TABLES]
SLOT_TABLE = [None] + ONEHOT_TABLES + GATHER_TABLES
GATHERED = len(GATHER_TABLES)
FIRST_GATHERED = 1 + ONEHOT
QUADS = (GATHERED + 3) // 4

SLOT = 32
PACK = P // SLOT
GROUP = 32
PRODUCTS = GROUP // PACK
GROUPS = P // GROUP
ROWS = (PACK - 1) * SLOT + NF
PAIR_CHUNKS = 4
COLS = PAIR_CHUNKS
BLOCKS = -(-NF // COLS)
REACH = BLOCKS // 2 + 1
H1, H2 = 512, 256
N1, N2 = H1 // P, H2 // P

def quad_slots(q):
    first = FIRST_GATHERED + 4 * q
    return range(first, min(first + 4, NF))


def plan_pieces():
    pieces, at = [], 0
    for _ in range(BLOCKS):
        columns, end = (at + REACH - 1) % BLOCKS, at + REACH
        while at < end:
            quadrant, first = divmod(at, BLOCKS)
            stop = min(BLOCKS, first + end - at)
            pieces.append((quadrant, first, stop, columns))
            at += stop - first
    return pieces


PIECES = plan_pieces()
PLACED = []
for depth in range(max(sum(p[0] == q for p in PIECES) for q in range(PACK))):
    for quadrant in range(PACK):
        here = [p for p in PIECES if p[0] == quadrant][::-1]
        if depth < len(here):
            under = max((n for n, p in enumerate(PLACED) if p[0] == quadrant), default=None)
            PLACED.append((quadrant, min(here[depth][2] * COLS, NF), here[depth][3], under))


def pair_place(a, b):
    for row, col in ((a, b), (b, a)):
        for quadrant, first, stop, columns in PIECES:
            if columns == col // COLS and first <= row // COLS < stop:
                return quadrant, col % COLS, row


ORDER = """
    q10 q11 g00 q12 g01 q13 g02 q14 g03
    g10 q20 a00 a01 g11 a02 a03 q21 g12 q22 g13 q23 b0
    q24 a10 g20 c0 a11 a12 g21 a13 q30 g22 q31 g23 b1
    q32 a20 a21 q33 a22 q34 a23 g30 c1 g31 g32 g33 b2
"""


def plan():
    steps = []
    for i in range(max(ONEHOT, QUADS)):
        if i < ONEHOT:
            steps.append(("onehot", 0, i))
        if i == 1:
            steps.append(("bottom", 0, 0))
        if 1 <= i <= QUADS:
            steps.append(("quad", 0, i - 1))
    names = {"q": "quad", "g": "gram", "a": "layer1", "b": "layer2", "c": "layer3"}
    steps += [(names[word[0]], int(word[1]), int(word[2:] or 0)) for word in ORDER.split()]
    return steps + [("last_layer1", LAST, 0), ("last_layer2", LAST, 0), ("layer3", LAST - 1, 0), ("last_layer3", LAST, 0)]


STEPS = plan()
TURNS = [s for s in STEPS if s[0] in ("bottom", "onehot", "quad")]
TURN_BANKS, GRAM_BANKS = 2, 4
BANK = [(n + TURN_BANKS) % (TURN_BANKS + GRAM_BANKS) if t == 0 else n % TURN_BANKS for n, (step, t, i) in enumerate(TURNS)]
BEFORE = [max((m for m in range(n) if BANK[m] == BANK[n]), default=None) for n in range(len(TURNS))]
BY_DVE = [t > 1 and n % 2 == 0 for n, (step, t, i) in enumerate(TURNS)]


DVE_SAMPLES, ACT_SAMPLES = (0, 1), (2, 3)


def moved(samples, groups):
    return groups * len(samples) * len(PLACED)


def turn(step, t, i):
    return TURNS.index((step, t, i))


def last_turn(t):
    return max(n for n, (step, u, q) in enumerate(TURNS) if u == t)


def build(nc, bottom, ids, ids_onehot, tables, w1_pairs, w1_bottom, b1, w2, b2, w3, out):
    ctx = ExitStack()
    with ctx:
        def sb(name, shape, dt=F32):
            return ctx.enter_context(nc.sbuf_tensor(name, shape, dt))

        def ps(name, shape, dt=F32):
            return ctx.enter_context(nc.psum_tensor(name, shape, dt))

        def sem(name):
            return ctx.enter_context(nc.semaphore(name))

        idx = sb("idx", [P, TILES, NTAB], I32)
        idb = sb("idb", [TP, RAWS, 2, B], I32)
        rowid = sb("rowid", [TP, CHUNKS // 2])
        raw = sb("raw", [TP, RAWS, CHUNKS, D])
        hi = sb("hi", [TP, SPLITS, CHUNKS, D], F32R)
        lo = sb("lo", [TP, SPLITS, CHUNKS, D], F32R)
        pick = sb("pick", [TP, CHUNKS // 2, 2, B], F32R)
        bot = sb("bot", [P, TILES, D])
        emb = sb("emb", [P, 2, GATHERED, D])
        embT = sb("embT", [P, B, SLOT])
        pairs = sb("pairs", [P, PAIR_CHUNKS, B])
        w1p = sb("w1p", [P, PAIR_CHUNKS, H1])
        w1b = sb("w1b", [P, H1])
        w2s = sb("w2s", [P, N1, H2])
        w3s = sb("w3s", [P, N2])
        b1s = sb("b1s", [P, N1])
        b2s = sb("b2s", [P, N2])
        h1 = sb("h1", [P, 2, N1, P])
        h2 = sb("h2", [P, 2, N2, P])
        y = sb("y", [1, B])
        ident = sb("ident", [P, P])
        scratch = sb("scratch", [P, 1])
        zeros = sb("zeros", [P, B], BF16)

        work_ps = ps("work_ps", [P, TURN_BANKS + GRAM_BANKS, 4, P])
        gram_ps = work_ps[:, TURN_BANKS:, :, :].rearrange("p b m w -> p (b m) w")
        h1_ps = ps("h1_ps", [P, N1, P])
        h2_ps = ps("h2_ps", [P, 4, P])
        last1 = [work_ps[:, b, 0, :] for b in range(N1)]
        last2 = [work_ps[:, N1 + n, 0, :] for n in range(N2)]
        last3 = gram_ps[0:1, 0, :]

        s_idx = sem("s_idx")
        s_idb = [sem(f"s_idb_{k}") for k in range(ONEHOT)]
        s_bottom = sem("s_bottom")
        s_raw = [sem(f"s_raw_{b}") for b in range(RAWS)]
        s_w1 = sem("s_w1")
        s_w2 = sem("s_w2")
        s_gather = [[sem(f"s_gather_{t}_{q}") for q in range(QUADS)] for t in range(TILES)]
        s_zeros = sem("s_zeros")
        s_ident0 = sem("s_ident0")
        s_ident = sem("s_ident")
        s_rowid = sem("s_rowid")
        s_pad = sem("s_pad")
        s_less = sem("s_less")
        s_hi = sem("s_hi")
        s_lo = sem("s_lo")
        s_pick = sem("s_pick")
        s_picked = sem("s_picked")
        s_turn = sem("s_turn")
        s_turnD = sem("s_turnD")
        s_turnA = sem("s_turnA")
        s_gram = sem("s_gram")
        s_pairD = sem("s_pairD")
        s_pairA = sem("s_pairA")
        s_h1mm = sem("s_h1mm")
        s_h1 = sem("s_h1")
        s_h2mm = sem("s_h2mm")
        s_h2 = sem("s_h2")
        s_ymm = sem("s_ymm")
        s_y = sem("s_y")
        s_last1mm = sem("s_last1mm")
        s_last1D = sem("s_last1D")
        s_last1A = sem("s_last1A")
        s_last2mm = sem("s_last2mm")
        s_last2D = sem("s_last2D")
        s_last2A = sem("s_last2A")
        s_out = sem("s_out")

        block = ctx.enter_context(nc.Block())

        def load_table(eng, k):
            f = ONEHOT_TABLES[k]
            src = tables[f].rearrange("(p c) d -> p c d", c=CHUNKS)
            whole = TP // 16 * 16
            eng.dma_start(raw[0:whole, k % RAWS], src[0:whole]).then_inc(s_raw[k % RAWS], 16)
            eng.dma_start(raw[whole:TP, k % RAWS], src[whole:TP]).then_inc(s_raw[k % RAWS], 16)

        def load_ids(eng, k):
            eng.dma_start(idb[:, k % RAWS, 0, :], ids_onehot[k].partition_broadcast(TP)).then_inc(s_idb[k], 16)

        def split_steps(k, c):
            return k + 2 if k else 1 + c // (CHUNKS // 4)

        @block.sync
        def _(sp):
            sp.dma_start(idx[:], ids.rearrange("(t p) f -> p t f", p=P)).then_inc(s_idx, 16)
            load_table(sp, 0)
            for k in range(1, ONEHOT):
                if k >= RAWS:
                    sp.wait_ge(s_pick, (k - RAWS + 1) * CHUNKS // 2)
                load_ids(sp, k)
                if k >= RAWS:
                    sp.wait_ge(s_lo, split_steps(k - RAWS, CHUNKS // 2 - 1))
                load_table(sp, k)
                if k == 1:
                    sp.dma_start(bot[:], bottom.rearrange("(t p) d -> p t d", p=P)).then_inc(s_bottom, 16)
            sp.wait_ge(s_turn, turn("onehot", 0, ONEHOT - 1))
            sp.dma_start(w1p[:], w1_pairs).then_inc(s_w1, 16)
            sp.dma_start(w1b[:], w1_bottom).then_inc(s_w1, 16)
            sp.dma_start(b1s[:], b1).then_inc(s_w1, 16)
            sp.dma_start(w2s[:], w2.rearrange("(k p) n -> p k n", p=P)).then_inc(s_w2, 16)
            sp.dma_start(b2s[:], b2).then_inc(s_w2, 16)
            sp.dma_start(w3s[:], w3).then_inc(s_w2, 16)
            sp.wait_ge(s_y, TILES)
            sp.dma_start(out.rearrange("b o -> o b"), y[:]).then_inc(s_out, 16)
            sp.wait_ge(s_out, 16)

        @block.gpsimd
        def _(pool):
            nc.gpsimd.memset(ident[:], 0.0).then_inc(s_ident0, 1)
            nc.gpsimd.iota(rowid[:], [[1, CHUNKS // 2]], base=0, channel_multiplier=CHUNKS,
                           allow_small_or_imprecise_dtypes=True).then_inc(s_rowid, 1)
            pool.wait_ge(s_ident0, 1)
            nc.gpsimd.affine_select(out=ident[:], in_=ident[:], compare_op=ALU.not_equal, fill=1.0, base=0,
                                    pattern=[[-1, P]], channel_multiplier=1).then_inc(s_ident, 1)
            pool.wait_ge(s_idx, 16)
            for t in range(TILES):
                for q in range(QUADS):
                    if t >= 2:
                        pool.wait_ge(s_turn, turn("quad", t - 2, q) + 1)
                    for slot in quad_slots(q):
                        f = SLOT_TABLE[slot]
                        pool.indirect_dma_start(
                            emb[:, t % 2, slot - FIRST_GATHERED, :], None, tables[f],
                            bass.IndirectOffsetOnAxis(ap=idx[:, t, f:f + 1], axis=0),
                        ).then_inc(s_gather[t][q], 16)

        def split_chunks(buf, k, step):
            halves = buf.rearrange("p (h c) d -> p h c d", h=2)
            return halves if k else halves[:, :, step * CHUNKS // 4:(step + 1) * CHUNKS // 4, :]

        def wait_emptied(eng, n):
            eng.wait_ge(s_turnD if BY_DVE[n] else s_turnA, BY_DVE[:n + 1].count(BY_DVE[n]))

        def wait_turns(eng, n):
            if True in BY_DVE[:n + 1]:
                eng.wait_ge(s_turnD, BY_DVE[:n + 1].count(True))
            eng.wait_ge(s_turnA, BY_DVE[:n + 1].count(False))

        @block.tensor
        def _(pe):
            def bank_free(n):
                if BEFORE[n] is not None:
                    wait_emptied(pe, BEFORE[n])

            def turn_bottom(n):
                bank_free(n)
                pe.wait_ge(s_bottom, 16)
                for t in range(TILES):
                    last = nc.tensor.transpose(work_ps[:, BANK[n], t, :], bot[:, t, :], ident[:])
                last.then_inc(s_turn, 1)

            def turn_quad(n, t, q):
                bank_free(n)
                slots = quad_slots(q)
                pe.wait_ge(s_gather[t][q], 16 * len(slots))
                for k, slot in enumerate(slots):
                    last = nc.tensor.transpose(work_ps[:, BANK[n], k, :], emb[:, t % 2, slot - FIRST_GATHERED, :], ident[:])
                last.then_inc(s_turn, 1)

            def onehot(n, k):
                bank_free(n)
                acc = work_ps[:, BANK[n], :, :].rearrange("p t b -> p (t b)")
                for c in range(CHUNKS // 2):
                    if c == 0 or k == 0:
                        pe.wait_ge(s_lo, split_steps(k, c))
                    pe.wait_ge(s_pick, k * CHUNKS // 2 + c + 1)
                    for half in range(2):
                        chunk = c + half * CHUNKS // 2
                        nc.tensor.matmul(acc, hi[:, k % SPLITS, chunk, :], pick[:, c, half, :],
                                         start=(c + half == 0), stop=False)
                        last = nc.tensor.matmul(acc, lo[:, k % SPLITS, chunk, :], pick[:, c, half, :],
                                                start=False, stop=(chunk == CHUNKS - 1))
                    if c < CHUNKS // 2 - 1:
                        last.then_inc(s_picked, 1)
                last.then_inc(s_turn, 1)

            def gram(t, h):
                g = GROUPS * t + h
                if h == 0:
                    wait_turns(pe, last_turn(t))
                if g == 0:
                    pe.wait_ge(s_pad, SLOT - NF + PAIR_CHUNKS)
                if g >= 2:
                    pe.wait_ge(s_pairD, moved(DVE_SAMPLES, g - 1))
                    pe.wait_ge(s_pairA, moved(ACT_SAMPLES, g - 1))
                for m in range(PRODUCTS):
                    b0 = t * P + h * GROUP + m * PACK
                    last = nc.tensor.matmul(gram_ps[0:ROWS, g % 2 * PRODUCTS + m, 0:PACK * NF],
                                            embT[:, b0:b0 + PACK, :].rearrange("p b s -> p (b s)")[:, 0:ROWS],
                                            embT[:, b0:b0 + PACK, 0:NF], start=True, stop=True)
                last.then_inc(s_gram, 1)

            def layer1_bottom(acc, t, n):
                nc.tensor.matmul(acc, w1b[:, n * P:(n + 1) * P], embT[:, t * P:(t + 1) * P, 0], start=True, stop=False)

            def layer1_pairs(acc, t, n):
                for c in range(PAIR_CHUNKS):
                    last = nc.tensor.matmul(acc, w1p[:, c, n * P:(n + 1) * P], pairs[:, c, t * P:(t + 1) * P],
                                            start=False, stop=(c == PAIR_CHUNKS - 1))
                return last

            def layer1(t, n):
                if n == 0:
                    if t == 0:
                        pe.wait_ge(s_w1, 48)
                    pe.wait_ge(s_pairD, moved(DVE_SAMPLES, GROUPS * (t + 1)))
                    pe.wait_ge(s_pairA, moved(ACT_SAMPLES, GROUPS * (t + 1)))
                    if t:
                        pe.wait_ge(s_h1, N1 * t)
                layer1_bottom(h1_ps[:, n, :], t, n)
                last = layer1_pairs(h1_ps[:, n, :], t, n)
                if n == N1 - 1:
                    last.then_inc(s_h1mm, 1)

            def layer2(t):
                if t == 0:
                    pe.wait_ge(s_w2, 48)
                pe.wait_ge(s_h1, N1 * (t + 1))
                if t:
                    pe.wait_ge(s_h2, N2 * t)
                    pe.wait_ge(s_y, t)
                for n in range(N2):
                    for k in range(N1):
                        last = nc.tensor.matmul(h2_ps[:, n, :], w2s[:, k, n * P:(n + 1) * P], h1[:, t % 2, k, :],
                                                start=(k == 0), stop=(k == N1 - 1))
                last.then_inc(s_h2mm, 1)

            def layer3(t):
                pe.wait_ge(s_h2, N2 * (t + 1))
                for k in range(N2):
                    last = nc.tensor.matmul(h2_ps[0:1, N2, :], w3s[:, k:k + 1], h2[:, t % 2, k, :],
                                            start=(k == 0), stop=(k == N2 - 1))
                last.then_inc(s_ymm, 1)

            pe.wait_ge(s_zeros, 1)
            for _ in range(WARM):
                nc.tensor.matmul(h1_ps[:, :, :].rearrange("p n b -> p (n b)"), zeros[:, 0:P], zeros[:],
                                 start=True, stop=True)

            pe.wait_ge(s_ident, 1)
            for step, t, i in STEPS:
                if step == "bottom":
                    turn_bottom(turn(step, t, i))
                if step == "onehot":
                    onehot(turn(step, t, i), i)
                if step == "quad":
                    turn_quad(turn(step, t, i), t, i)
                if step == "gram":
                    gram(t, i)
                if step == "layer1":
                    layer1(t, i)
                if step == "layer2":
                    layer2(t)
                if step == "layer3":
                    layer3(t)
                if step == "last_layer1":
                    pe.wait_ge(s_pairD, moved(DVE_SAMPLES, GROUPS * TILES - 1))
                    pe.wait_ge(s_pairA, moved(ACT_SAMPLES, GROUPS * TILES - 1))
                    for n in range(N1):
                        layer1_bottom(last1[n], t, n)
                    pe.wait_ge(s_pairD, moved(DVE_SAMPLES, GROUPS * TILES))
                    pe.wait_ge(s_pairA, moved(ACT_SAMPLES, GROUPS * TILES))
                    for n in range(N1):
                        layer1_pairs(last1[n], t, n).then_inc(s_last1mm, 1)
                if step == "last_layer2":
                    for k in range(N1):
                        pe.wait_ge(s_last1A if k % 2 else s_last1D, k // 2 + 1)
                        for n in range(N2):
                            last = nc.tensor.matmul(last2[n], w2s[:, k, n * P:(n + 1) * P], h1[:, t % 2, k, :],
                                                    start=(k == 0), stop=(k == N1 - 1))
                            if k == N1 - 1:
                                last.then_inc(s_last2mm, 1)
                if step == "last_layer3":
                    for k in range(N2):
                        pe.wait_ge(s_last2A if k % 2 else s_last2D, 1)
                        last = nc.tensor.matmul(last3, w3s[:, k:k + 1], h2[:, t % 2, k, :],
                                                start=(k == 0), stop=(k == N2 - 1))
                    last.then_inc(s_ymm, 1)

        def move_turned(copy, n, step, t, i, done):
            if step == "bottom":
                src, dst = work_ps[:, BANK[n], :, :].rearrange("p t b -> p (t b)"), embT[:, :, 0]
            elif step == "onehot":
                src, dst = work_ps[:, BANK[n], :, :].rearrange("p t b -> p (t b)"), embT[:, :, 1 + i]
            else:
                slots = quad_slots(i)
                src = work_ps[:, BANK[n], 0:len(slots), :]
                dst = embT[:, t * P:(t + 1) * P, slots[0]:slots[-1] + 1].rearrange("p b s -> p s b")
            copy(dst, src).then_inc(done, 1)

        def move_pairs(eng, copy, t, h, samples, done):
            b0 = t * P + h * GROUP
            first = (GROUPS * t + h) % 2 * PRODUCTS
            before = moved(samples, GROUPS * t + h)
            for n, (quadrant, rows, block, under) in enumerate(PLACED):
                cols = min(COLS, NF - block * COLS)
                for k, s in enumerate(samples):
                    if under is not None:
                        eng.wait_ge(done, before + under * len(samples) + k + 1)
                    at = s * NF + block * COLS
                    src = gram_ps[s * SLOT:s * SLOT + rows, first:first + PRODUCTS, at:at + cols]
                    dst = pairs[quadrant * SLOT:quadrant * SLOT + rows, 0:cols, b0 + s:b0 + GROUP:PACK]
                    copy(dst.rearrange("p g m -> p m g"), src).then_inc(done, 1)

        @block.vector
        def _(dve):
            def one_hot(k, first, end):
                dve.wait_ge(s_less, k + 1)
                for c in range(first, end):
                    if k:
                        if c < CHUNKS // 2 - 1:
                            dve.wait_ge(s_picked, (k - 1) * (CHUNKS // 2 - 1) + c + 1)
                        else:
                            dve.wait_ge(s_turn, turn("onehot", 0, k - 1) + 1)
                    nc.vector.tensor_scalar(pick[:, c], idb[:, k % RAWS], rowid[:, c:c + 1], None,
                                            ALU.is_equal).then_inc(s_pick, 1)

            def low_parts(k, step=0):
                dve.wait_ge(s_hi, split_steps(k, 0) + step)
                nc.vector.tensor_tensor(split_chunks(lo[:, k % SPLITS], k, step), split_chunks(raw[:, k % RAWS], k, step),
                                        split_chunks(hi[:, k % SPLITS], k, step), ALU.subtract).then_inc(s_lo, 1)

            nc.vector.memset(zeros[:], 0.0).then_inc(s_zeros, 1)
            dve.wait_ge(s_rowid, 1)
            one_hot(0, 0, 2)
            low_parts(0)
            low_parts(0, 1)
            one_hot(0, 2, CHUNKS // 2)
            for step, t, i in STEPS:
                if step == "onehot" and i + 1 < ONEHOT:
                    one_hot(i + 1, 0, 1)
                    low_parts(i + 1)
                    one_hot(i + 1, 1, CHUNKS // 2)
                if step in ("bottom", "onehot", "quad"):
                    n = turn(step, t, i)
                    if BY_DVE[n]:
                        dve.wait_ge(s_turn, n + 1)
                        move_turned(nc.vector.tensor_copy, n, step, t, i, s_turnD)
                if step == "gram":
                    dve.wait_ge(s_gram, GROUPS * t + i + 1)
                    move_pairs(dve, nc.vector.tensor_copy, t, i, DVE_SAMPLES, s_pairD)
                if step == "last_layer1":
                    for n in range(0, N1, 2):
                        dve.wait_ge(s_last1mm, n + 1)
                        nc.vector.tensor_scalar(h1[:, t % 2, n, :], last1[n], b1s[:, n:n + 1], 0.0,
                                                ALU.add, ALU.max).then_inc(s_last1D, 1)
                if step == "last_layer2":
                    dve.wait_ge(s_last2mm, 1)
                    nc.vector.tensor_scalar(h2[:, t % 2, 0, :], last2[0], b2s[:, 0:1], 0.0,
                                            ALU.add, ALU.max).then_inc(s_last2D, 1)
                if step == "last_layer3":
                    dve.wait_ge(s_ymm, TILES)
                    nc.vector.tensor_copy(y[:, t * P:(t + 1) * P], last3).then_inc(s_y, 1)

        @block.scalar
        def _(act):
            load_ids(act, 0)
            act.wait_ge(s_zeros, 1)
            nc.scalar.copy(scratch[:], zeros[:, 0:1])

            def less(k):
                act.wait_ge(s_idb[k], 16)
                if k >= RAWS:
                    act.wait_ge(s_pick, (k - RAWS + 1) * CHUNKS // 2)
                nc.scalar.activation(idb[:, k % RAWS, 1, :], idb[:, k % RAWS, 0, :], ACT.Copy,
                                     bias=-float(CHUNKS // 2)).then_inc(s_less, 1)

            def high_parts(k, step=0):
                if k >= SPLITS:
                    act.wait_ge(s_turn, turn("onehot", 0, k - SPLITS) + 1)
                act.wait_ge(s_raw[k % RAWS], 32 * (k // RAWS + 1))
                nc.scalar.copy(split_chunks(hi[:, k % SPLITS], k, step),
                               split_chunks(raw[:, k % RAWS], k, step)).then_inc(s_hi, 1)

            less(0)
            high_parts(0)
            high_parts(0, 1)
            for k in range(1, AHEAD):
                less(k)
                high_parts(k)
            padding = [embT[:, :, slot] for slot in range(NF, SLOT)] + [pairs[:, c, :] for c in range(PAIR_CHUNKS)]
            for step, t, i in STEPS:
                if step == "onehot" and i + AHEAD < ONEHOT:
                    less(i + AHEAD)
                    high_parts(i + AHEAD)
                if step in ("bottom", "onehot", "quad"):
                    n = turn(step, t, i)
                    if not BY_DVE[n]:
                        act.wait_ge(s_turn, n + 1)
                        move_turned(nc.scalar.copy, n, step, t, i, s_turnA)
                    if n < len(padding):
                        nc.scalar.copy(padding[n], zeros[:]).then_inc(s_pad, 1)
                if step == "gram":
                    act.wait_ge(s_gram, GROUPS * t + i + 1)
                    move_pairs(act, nc.scalar.copy, t, i, ACT_SAMPLES, s_pairA)
                if step == "layer1" and i == N1 - 1:
                    act.wait_ge(s_h1mm, t + 1)
                    for n in range(N1):
                        nc.scalar.activation(h1[:, t % 2, n, :], h1_ps[:, n, :], ACT.Relu,
                                             bias=b1s[:, n:n + 1]).then_inc(s_h1, 1)
                if step == "layer2":
                    act.wait_ge(s_h2mm, t + 1)
                    for n in range(N2):
                        nc.scalar.activation(h2[:, t % 2, n, :], h2_ps[:, n, :], ACT.Relu,
                                             bias=b2s[:, n:n + 1]).then_inc(s_h2, 1)
                if step == "layer3":
                    act.wait_ge(s_ymm, t + 1)
                    nc.scalar.copy(y[:, t * P:(t + 1) * P], h2_ps[0:1, N2, :]).then_inc(s_y, 1)
                if step == "last_layer1":
                    for n in range(1, N1, 2):
                        act.wait_ge(s_last1mm, n + 1)
                        nc.scalar.activation(h1[:, t % 2, n, :], last1[n], ACT.Relu,
                                             bias=b1s[:, n:n + 1]).then_inc(s_last1A, 1)
                if step == "last_layer2":
                    act.wait_ge(s_last2mm, 2)
                    nc.scalar.activation(h2[:, t % 2, 1, :], last2[1], ACT.Relu,
                                         bias=b2s[:, 1:2]).then_inc(s_last2A, 1)


def kernel(**inputs):
    import numpy as np
    import concourse.bacc as bacc
    from concourse.bass_utils import run_bass_kernel_spmd

    feature = [0] + [f + 1 for f in SLOT_TABLE[1:]]
    w1 = np.asarray(inputs["W_top1"])
    w1_pairs = np.zeros((P, PAIR_CHUNKS, H1), w1.dtype)
    for b in range(NF):
        for a in range(b):
            low, high = sorted((feature[a], feature[b]))
            quadrant, chunk, row = pair_place(a, b)
            w1_pairs[SLOT * quadrant + row, chunk] = w1[low * NF - low * (low + 1) // 2 + high - low - 1]
    laid = {
        "bottom": inputs["r_bottom_output"],
        "ids": inputs["ids"],
        "ids_onehot": np.asarray(inputs["ids"])[:, ONEHOT_TABLES].T,
        "w1_pairs": w1_pairs,
        "w1_bottom": w1[PAIRS:],
        "b1": np.asarray(inputs["b_top1"]).reshape(N1, P).T,
        "w2": inputs["W_top2"],
        "b2": np.asarray(inputs["b_top2"]).reshape(N2, P).T,
        "w3": np.asarray(inputs["W_top3"]).reshape(N2, P).T,
    }
    for f in range(NTAB):
        laid[f"tbl_{f}"] = inputs[f"tbl_{f}"]

    nc = bacc.Bacc("TRN2", target_bir_lowering=False, num_devices=1)
    arrays, aps = {}, {}
    for name, a in laid.items():
        a = np.ascontiguousarray(a)
        arrays[f"in_{name}"] = a
        aps[name] = nc.dram_tensor(f"in_{name}", a.shape, mybir.dt.from_np(a.dtype), kind="ExternalInput").ap()
    out = nc.dram_tensor("out_y", (B, 1), F32, kind="ExternalOutput").ap()
    build(nc, aps["bottom"], aps["ids"], aps["ids_onehot"], [aps[f"tbl_{f}"] for f in range(NTAB)], aps["w1_pairs"],
          aps["w1_bottom"], aps["b1"], aps["w2"], aps["b2"], aps["w3"], out)
    r = run_bass_kernel_spmd(nc, [arrays], core_ids=[0])
    return r.results[0]["out_y"]
```
